# Optimizing a Trainium2 kernel written in Bass

```python
import numpy as np
import jax
import jax.numpy as jnp

def _softmax(x, axis=-1):
    return jax.nn.softmax(x, axis=axis)

def _gelu(x):
    return jax.nn.gelu(x, approximate=True)

def _silu(x):
    return jax.nn.silu(x)

def _sigmoid(x):
    return jax.nn.sigmoid(x)

def _layernorm(x, axis=-1, eps=1e-05):
    m = jnp.mean(x, axis=axis, keepdims=True)
    v = jnp.var(x, axis=axis, keepdims=True)
    return (x - m) / jnp.sqrt(v + eps)

def _scatter_add(tgt, idx, src, axis=0):
    return tgt.at[idx].add(src)

def _segment_sum(src, seg, n):
    return jax.ops.segment_sum(src, seg, n)
kernel_name = 'mk_cond_resid_d4_seqx_r4_d0f3f7'

def setup_inputs(seed: int=0):
    np.random.seed(seed)
    _w = jnp.asarray

    def _rec_inputs():
        import jax
        import jax.numpy as jnp
        _rk = jax.random.key(seed)
        x = 7.22e-05 + 1 * jax.random.normal(jax.random.fold_in(_rk, 1), (8, 512, 256), jnp.float32)
        _lenS = 512 - jax.random.randint(jax.random.fold_in(_rk, 7), (8,), 0, max(1, 512 // 4) + 1, jnp.int32)
        _lenS2 = 512 - jax.random.randint(jax.random.fold_in(_rk, 8), (8,), 0, max(1, 512 // 4) + 1, jnp.int32)
        cond_8 = jax.random.uniform(jax.random.fold_in(_rk, 11), (8, 8), jnp.float32, 0.0, 0.999837)
        return (x, cond_8)
    x, cond_8 = _rec_inputs()

    def _L0_cond_setup():
        import jax, jax.numpy as jnp
        import numpy as np
        key = jax.random.key(seed)
        k1, k2, k3, k4, k5 = jax.random.split(key, 5)
        B, N, T, O, G = (32, 64, 256, 256, 8)
        x = jax.random.normal(k1, (B, N, T), dtype=jnp.float32)
        y = jax.random.uniform(k2, (B, G), dtype=jnp.float32)
        weight = jax.random.normal(k3, (G, O, T), dtype=jnp.float32) * (1.0 / np.sqrt(T))
        mask = jax.random.uniform(k4, (O, T), dtype=jnp.float32)
        bias = jax.random.normal(k5, (O,), dtype=jnp.float32)
        return {'x': x, 'y': y, 'weight': weight, 'mask': mask, 'bias': bias}
    _L0_cond_all = _L0_cond_setup()
    _L0_cond_in = {k: v for k, v in _L0_cond_all.items() if k in ('weight', 'mask', 'bias')}
    del _L0_cond_all

    def _L1_cond_setup():
        import jax, jax.numpy as jnp
        import numpy as np
        B, S, D = (16, 512, 256)
        E, H = (8, 512)
        key = jax.random.key(seed)
        ks = jax.random.split(key, 8)
        scale = 0.02
        x = jax.random.normal(ks[0], (B, S, D), dtype=jnp.float32)
        opcode_onehot = jax.random.uniform(ks[1], (B, E), dtype=jnp.float32)
        W_up = jax.random.normal(ks[2], (E, H, D), dtype=jnp.float32) * scale
        b_up = jnp.zeros((E, H), dtype=jnp.float32)
        W_gate = jax.random.normal(ks[3], (E, H, D), dtype=jnp.float32) * scale
        b_gate = jnp.zeros((E, H), dtype=jnp.float32)
        W_down = jax.random.normal(ks[4], (E, D, H), dtype=jnp.float32) * scale
        b_down = jnp.zeros((E, D), dtype=jnp.float32)
        return {'x': x, 'opcode_onehot': opcode_onehot, 'W_up': W_up, 'b_up': b_up, 'W_gate': W_gate, 'b_gate': b_gate, 'W_down': W_down, 'b_down': b_down}
    _L1_cond_all = _L1_cond_setup()
    _L1_cond_in = {k: v for k, v in _L1_cond_all.items() if k in ('W_up', 'b_up', 'W_gate', 'b_gate', 'W_down', 'b_down')}
    del _L1_cond_all

    def _L2_cond_setup():
        import jax, jax.numpy as jnp
        import numpy as np
        TOP_K = 2
        NUM_MOE_LAYERS = 12

        def _gemma_mlp(x, gate_w, up_w, down_w):
            g = jnp.einsum('bsh,hi->bsi', x, gate_w)
            u = jnp.einsum('bsh,hi->bsi', x, up_w)
            return jnp.einsum('bsi,ih->bsh', jax.nn.gelu(g, approximate=True) * u, down_w)
        key = jax.random.key(seed)
        ks = jax.random.split(key, 8)
        B, S, H, I, E = (32, 64, 256, 1024, 8)
        std = 0.02
        return {'x': jax.random.normal(ks[0], (B, S, H), jnp.float32), 'router_logits': jax.random.normal(ks[1], (B, E), jnp.float32), 'skill_gate': jax.random.normal(ks[2], (E, H, I), jnp.float32) * std, 'skill_up': jax.random.normal(ks[3], (E, H, I), jnp.float32) * std, 'skill_down': jax.random.normal(ks[4], (E, I, H), jnp.float32) * std, 'shared_gate': jax.random.normal(ks[5], (H, I), jnp.float32) * std, 'shared_up': jax.random.normal(ks[6], (H, I), jnp.float32) * std, 'shared_down': jax.random.normal(ks[7], (I, H), jnp.float32) * std}
    _L2_cond_all = _L2_cond_setup()
    _L2_cond_in = {k: v for k, v in _L2_cond_all.items() if k in ('skill_gate', 'skill_up', 'skill_down', 'shared_gate', 'shared_up', 'shared_down')}
    del _L2_cond_all

    def _L3_cond_setup():
        import jax, jax.numpy as jnp
        import numpy as np
        R = 16
        ALPHA = 32.0
        SCALING = ALPHA / R
        key = jax.random.key(seed)
        ks = jax.random.split(key, 6)
        B, T, C, O, E = (16, 375, 256, 256, 8)
        x = jax.random.normal(ks[0], (B, T, C), dtype=jnp.float32)
        w = jax.random.uniform(ks[1], (B, E), dtype=jnp.float32)
        W_base = jax.random.normal(ks[2], (O, C), dtype=jnp.float32) * 0.02
        b_base = jax.random.normal(ks[3], (O,), dtype=jnp.float32) * 0.02
        As = jax.random.normal(ks[4], (E, R, C), dtype=jnp.float32) * 0.02
        Bs = jax.random.normal(ks[5], (E, O, R), dtype=jnp.float32) * 0.02
        return {'x': x, 'w': w, 'W_base': W_base, 'b_base': b_base, 'As': As, 'Bs': Bs}
    _L3_cond_all = _L3_cond_setup()
    _L3_cond_in = {k: v for k, v in _L3_cond_all.items() if k in ('W_base', 'b_base', 'As', 'Bs')}
    del _L3_cond_all
    return {'x': x, 'cond_8': cond_8, 'L0_cond_weight': _L0_cond_in['weight'], 'L0_cond_mask': _L0_cond_in['mask'], 'L0_cond_bias': _L0_cond_in['bias'], 'L1_cond_W_up': _L1_cond_in['W_up'], 'L1_cond_b_up': _L1_cond_in['b_up'], 'L1_cond_W_gate': _L1_cond_in['W_gate'], 'L1_cond_b_gate': _L1_cond_in['b_gate'], 'L1_cond_W_down': _L1_cond_in['W_down'], 'L1_cond_b_down': _L1_cond_in['b_down'], 'L2_cond_skill_gate': _L2_cond_in['skill_gate'], 'L2_cond_skill_up': _L2_cond_in['skill_up'], 'L2_cond_skill_down': _L2_cond_in['skill_down'], 'L2_cond_shared_gate': _L2_cond_in['shared_gate'], 'L2_cond_shared_up': _L2_cond_in['shared_up'], 'L2_cond_shared_down': _L2_cond_in['shared_down'], 'L3_cond_W_base': _L3_cond_in['W_base'], 'L3_cond_b_base': _L3_cond_in['b_base'], 'L3_cond_As': _L3_cond_in['As'], 'L3_cond_Bs': _L3_cond_in['Bs']}

def reference(x, cond_8, L0_cond_weight, L0_cond_mask, L0_cond_bias, L1_cond_W_up, L1_cond_b_up, L1_cond_W_gate, L1_cond_b_gate, L1_cond_W_down, L1_cond_b_down, L2_cond_skill_gate, L2_cond_skill_up, L2_cond_skill_down, L2_cond_shared_gate, L2_cond_shared_up, L2_cond_shared_down, L3_cond_W_base, L3_cond_b_base, L3_cond_As, L3_cond_Bs):
    import jax
    import jax.numpy as jnp

    def _L0_cond_ref(x, y, weight, mask, bias):
        import jax, jax.numpy as jnp
        import numpy as np
        masked_w = weight * mask[None, :, :]
        w_bot = jnp.einsum('bg,got->bot', y, masked_w)
        return jnp.einsum('bnt,bot->bno', x, w_bot) + bias

    def _L1_cond_ref(x, opcode_onehot, W_up, b_up, W_gate, b_gate, W_down, b_down):
        import jax, jax.numpy as jnp
        import numpy as np
        B, S, D = (16, 512, 256)
        E, H = (8, 512)
        expert = jnp.argmax(opcode_onehot, axis=-1)
        wu, bu = (W_up[expert], b_up[expert])
        wg, bg = (W_gate[expert], b_gate[expert])
        wd, bd = (W_down[expert], b_down[expert])
        up = jnp.einsum('bsd,bhd->bsh', x, wu) + bu[:, None, :]
        gate = jnp.einsum('bsd,bhd->bsh', x, wg) + bg[:, None, :]
        hidden = jax.nn.silu(up) * gate
        out = jnp.einsum('bsh,bdh->bsd', hidden, wd) + bd[:, None, :]
        return out

    def _L2_cond_ref(x, router_logits, skill_gate, skill_up, skill_down, shared_gate, shared_up, shared_down):
        import jax, jax.numpy as jnp
        import numpy as np
        TOP_K = 2
        NUM_MOE_LAYERS = 12

        def _gemma_mlp(x, gate_w, up_w, down_w):
            g = jnp.einsum('bsh,hi->bsi', x, gate_w)
            u = jnp.einsum('bsh,hi->bsi', x, up_w)
            return jnp.einsum('bsi,ih->bsh', jax.nn.gelu(g, approximate=True) * u, down_w)
        B = x.shape[0]
        E = skill_gate.shape[0]
        rw = jax.nn.softmax(router_logits.astype(jnp.float32), axis=-1)
        w, sel = jax.lax.top_k(rw, TOP_K)
        w = w / w.sum(axis=-1, keepdims=True)
        w = w.astype(x.dtype)
        scale = 1.0 / NUM_MOE_LAYERS
        w = scale * w + (1.0 - scale) * jax.lax.stop_gradient(w)
        dense_w = jnp.zeros((B, E), x.dtype).at[jnp.arange(B)[:, None], sel].add(w)

        def step(acc, params):
            g, u, d, we = params
            return (acc + we[:, None, None] * _gemma_mlp(x, g, u, d), None)
        out, _ = jax.lax.scan(step, jnp.zeros_like(x), (skill_gate, skill_up, skill_down, dense_w.T))
        out = out + _gemma_mlp(x, shared_gate, shared_up, shared_down)
        return out

    def _L3_cond_ref(x, w, W_base, b_base, As, Bs):
        import jax, jax.numpy as jnp
        import numpy as np
        R = 16
        ALPHA = 32.0
        SCALING = ALPHA / R
        out = jnp.einsum('btc,oc->bto', x, W_base) + b_base
        h = jnp.einsum('btc,erc->bter', x, As)
        lora = jnp.einsum('bter,eor,be->bto', h, Bs, w)
        return out + lora * SCALING
    x = x + _L0_cond_ref(x, cond_8, L0_cond_weight, L0_cond_mask, L0_cond_bias)
    x = x + _L1_cond_ref(x, cond_8, L1_cond_W_up, L1_cond_b_up, L1_cond_W_gate, L1_cond_b_gate, L1_cond_W_down, L1_cond_b_down)
    x = x + _L2_cond_ref(x, cond_8, L2_cond_skill_gate, L2_cond_skill_up, L2_cond_skill_down, L2_cond_shared_gate, L2_cond_shared_up, L2_cond_shared_down)
    x = x + _L3_cond_ref(x, cond_8, L3_cond_W_base, L3_cond_b_base, L3_cond_As, L3_cond_Bs)
    return x

_drawn_inputs = setup_inputs


def setup_inputs(seed=0):
    import zlib

    import numpy as np

    out = dict(_drawn_inputs(seed))
    spreads = {'L1_cond_b_up': (0.0, 0.8), 'L1_cond_b_gate': (0.0, 0.8), 'L1_cond_b_down': (0.0, 0.1)}
    factors = {'L3_cond_b_base': 5.588}
    for name, (base, spread) in spreads.items():
        noise = np.random.default_rng([zlib.crc32(name.encode()), seed]).standard_normal(out[name].shape)
        drawn = base * np.exp(spread * noise) if base else spread * noise
        out[name] = jnp.asarray(drawn.astype(out[name].dtype))
    for name, factor in factors.items():
        out[name] = (out[name] * factor).astype(out[name].dtype)
    return out
```

```python
from contextlib import ExitStack

import concourse.bass as bass
from concourse import mybir

P = 128
BATCH, TOKENS, DIM = 8, 512, 256
EXPERTS = 8
CT = DIM // P
TOP_K = 2
SWIGLU_TILES = 512 // P
GEGLU_TILES = 1024 // P
TILE_W = 2 * CT * P + DIM
CHUNK = 2
RAW_SLOTS = 4
RING = 4
GROUP = P // EXPERTS
LORA_R = 16
LORA_SCALING = 32.0 / LORA_R
N_BIAS = 2 * SWIGLU_TILES + CT
NUM_MOE_LAYERS = 12
LAST = BATCH - 1

F32 = mybir.dt.float32
F32R = mybir.dt.float32r
U32 = mybir.dt.uint32
ALU = mybir.AluOpType
ACT = mybir.ActivationFunctionType
AX_X = mybir.AxisListType.X

SWIGLU, GEGLU = 0, 1
TILES = (SWIGLU_TILES, (TOP_K + 1) * GEGLU_TILES)
OWN = (SWIGLU_TILES, TOP_K * GEGLU_TILES)


def is_shared(layer, j):
    return layer == GEGLU and j % 3 == 2


def own_index(layer, j):
    return j if layer == SWIGLU else j - j // 3


def tile_no(layer, b, j):
    return TILES[SWIGLU] * b + j if layer == SWIGLU else TILES[SWIGLU] * BATCH + TILES[GEGLU] * b + j


def own_no(layer, b, s):
    return OWN[SWIGLU] * b + s if layer == SWIGLU else OWN[SWIGLU] * BATCH + OWN[GEGLU] * b + s


def sample_no(layer, b):
    return BATCH * layer + b


def is_at(b, n):
    return isinstance(b, int) and b == n


def ahead(layer, b, parity, j, k):
    j += k
    if j < TILES[layer]:
        return layer, b, parity, j
    j -= TILES[layer]
    if not is_at(b, LAST):
        return layer, b + 1, 1 - parity, j
    return (GEGLU, 0, 0, j) if layer == SWIGLU else None


def ring_predecessor(layer, b, s):
    s -= RING
    if s < 0:
        if is_at(b, 0):
            if layer == SWIGLU:
                return None
            layer, b = SWIGLU, LAST
        else:
            b = b - 1
        s += OWN[layer]
    j = s if layer == SWIGLU else s + s // 2
    return layer, b, j


def raw_place(layer, b, parity, s):
    n = s // CHUNK
    if layer == SWIGLU:
        return OWN[SWIGLU] // CHUNK * parity + n, 16 // 2 * (b - parity) + 16
    rounds = OWN[GEGLU] // CHUNK // RAW_SLOTS
    return n % RAW_SLOTS, 16 * (BATCH // 2 + n // RAW_SLOTS + 1 + rounds * b)


def wait(engine, semaphore, value):
    if isinstance(value, int) and value <= 0:
        return
    engine.wait_ge(semaphore, value)


def for_samples(engine, step):
    step(0, 0)
    with engine.Fori(0, (BATCH - 2) // 2) as i:
        step(2 * i + 1, 1)
        step(2 * i + 2, 0)
    step(LAST, LAST % 2)


def build(nc, x_in, cond_in, cond_rows_in, select_in, mix_w_in, mask_in, mix_bias_in, swiglu_w_in,
          swiglu_bias_in, geglu_w_in, shared_w_in, base_in, base_bias_in, lora_a_in, lora_b_in, out):
    with ExitStack() as ctx:
        def sb(name, shape, dt=F32):
            return ctx.enter_context(nc.sbuf_tensor(name, shape, dt))

        def sem(name):
            return ctx.enter_context(nc.semaphore(name))

        x = sb("x", [P, BATCH, CT, TOKENS])
        xs_hi = sb("xs_hi", [P, 2, CT, TOKENS], F32R)
        xs_lo = sb("xs_lo", [P, 2, CT, TOKENS], F32R)
        xm_hi = sb("xm_hi", [P, CT, TOKENS], F32R)
        xm_lo = sb("xm_lo", [P, CT, TOKENS], F32R)
        raw = sb("raw", [P, (RAW_SLOTS + 1) * CHUNK * TILE_W])
        raw_chunk = raw[:, :].rearrange("p (c w) -> p c w", w=CHUNK * TILE_W)
        mix_w_cols = DIM // GROUP * DIM
        mix_w = raw[:, (RAW_SLOTS + 1) * CHUNK * TILE_W - mix_w_cols:].rearrange("p (c t) -> p c t", t=DIM)
        ring_hi = sb("ring_hi", [P, RING, TILE_W], F32R)
        ring_lo = sb("ring_lo", [P, RING, TILE_W], F32R)
        shared_hi = sb("shared_hi", [P, GEGLU_TILES // CHUNK, CHUNK * TILE_W], F32R)
        shared_lo = sb("shared_lo", [P, GEGLU_TILES // CHUNK, CHUNK * TILE_W], F32R)
        own_w = sb("own_w", [P, CT, BATCH, DIM])
        wm_hi = sb("wm_hi", [P, CT, DIM], F32R)
        wm_lo = sb("wm_lo", [P, CT, DIM], F32R)
        gated = sb("gated", [P, 2, TOKENS])
        hidden = sb("hidden", [P, 2, TOKENS])
        hidden_hi = sb("hidden_hi", [P, 2, TOKENS], F32R)
        hidden_lo = sb("hidden_lo", [P, 2, TOKENS], F32R)
        mask = sb("mask", [P, CT, DIM])
        lora_b_scaled = mask[:, :, :]
        base = sb("base", [P, CT, DIM])
        lora_a = sb("lora_a", [P, DIM])
        lora_b = sb("lora_b", [P, DIM])
        select = sb("select", [P, GROUP])
        cond_rows = sb("cond_rows", [P, BATCH])
        mixer = sb("mixer", [P, BATCH, GROUP])
        mix_bias = sb("mix_bias", [P, CT])
        base_bias = sb("base_bias", [P, CT])
        swiglu_bias = sb("swiglu_bias", [P, BATCH, N_BIAS])
        cond = sb("cond", [P, BATCH, EXPERTS])
        ranked = sb("ranked", [P, BATCH, EXPERTS])
        ranks = sb("ranks", [P, BATCH, EXPERTS], U32)
        soft = sb("soft", [P, BATCH, EXPERTS])
        total = sb("total", [P, BATCH])
        top_w = sb("top_w", [P, BATCH, TOP_K])
        top_part = sb("top_part", [P, BATCH, TOP_K])

        ps = {name: ctx.enter_context(nc.psum_tensor(name, [P, 2, TOKENS], F32))
              for name in ("ps_first", "ps_second", "ps_out", "ps_mix")}
        ps_first, ps_second, ps_out, ps_mix = (ps[n] for n in ("ps_first", "ps_second", "ps_out", "ps_mix"))

        cond_landed, rows_landed, mask_landed, consts_landed = map(
            sem, ("cond_landed", "rows_landed", "mask_landed", "consts_landed"))
        mix_w_landed = [sem(f"mix_w_landed{i}") for i in range(4)]
        x_landed = [sem(f"x_landed{i}") for i in range(4)]
        bias_landed = sem("bias_landed")
        raw_landed = [sem(f"raw_landed{i}") for i in range(RAW_SLOTS)]
        shared_landed = sem("shared_landed")
        stored = sem("stored")
        route = sem("route")
        soft_ready = sem("soft_ready")
        mixer_ready = sem("mixer_ready")
        own_made = sem("own_made")
        own_ready = sem("own_ready")
        lora_scaled = sem("lora_scaled")
        lora_made = sem("lora_made")
        lora_ready = sem("lora_ready")
        mix_hi, mix_lo, mix_done, mix_added = map(sem, ("mix_hi", "mix_lo", "mix_done", "mix_added"))
        xs_hi_done, xs_lo_done, out_added = map(sem, ("xs_hi_done", "xs_lo_done", "out_added"))
        first_done, second_done, gated_done, hidden_done, hid_hi_done, hid_lo_done, down_done = map(
            sem, ("first_done", "second_done", "gated_done", "hidden_done", "hid_hi_done",
                  "hid_lo_done", "down_done"))
        ring_hi_done, ring_lo_done = map(sem, ("ring_hi_done", "ring_lo_done"))
        shared_hi_done, shared_lo_done = map(sem, ("shared_hi_done", "shared_lo_done"))

        LORA_PAIRS = BATCH // 2
        OWN_GROUPS = CT * 4
        block = ctx.enter_context(nc.Block())

        @block.sync
        def _(sp):
            sp.dma_start(cond[:, :, :], cond_in).then_inc(cond_landed, 16)
            quarter = DIM // GROUP // 4
            for i in range(4):
                sp.dma_start(mix_w[:, quarter * i:quarter * (i + 1), :],
                             mix_w_in[:, quarter * i:quarter * (i + 1), :]).then_inc(mix_w_landed[i], 16)
            sp.dma_start(x[:, 0], x_in[0]).then_inc(x_landed[0], 16)

            def expert(b, k):
                return sp.value_load(ranks[0:1, b, k:k + 1], min_val=0, max_val=EXPERTS - 1)

            def load_swiglu(b, half):
                e = expert(b, 0)
                for q in range(SWIGLU_TILES // CHUNK):
                    slot = (SWIGLU_TILES // CHUNK) * half + q
                    wait(sp, ring_lo_done, own_no(SWIGLU, b, CHUNK * (q + 1)) - CHUNK * RAW_SLOTS)
                    sp.dma_start(raw_chunk[:, slot, :], swiglu_w_in[e, q]).then_inc(raw_landed[slot], 16)

            def load_shared(i):
                wait(sp, shared_lo_done, i)
                sp.dma_start(raw_chunk[:, RAW_SLOTS, :], shared_w_in[i]).then_inc(shared_landed, 16)

            sp.wait_ge(route, 2 * BATCH)
            load_swiglu(0, 0)
            with sp.Fori(0, BATCH) as b:
                sp.dma_start(swiglu_bias[:, b, :], swiglu_bias_in[expert(b, 0)]).then_inc(bias_landed, 16)
            sp.dma_start(x[:, 1], x_in[1]).then_inc(x_landed[1], 16)
            sp.dma_start(x[:, 2], x_in[2]).then_inc(x_landed[2], 16)
            sp.wait_ge(own_made, OWN_GROUPS)
            load_swiglu(1, 1)
            sp.dma_start(x[:, 3:], x_in[3:].rearrange("b p c t -> p b c t")).then_inc(x_landed[3], 16)
            load_shared(0)
            with sp.Fori(1, BATCH // 2) as pair:
                load_swiglu(2 * pair, 0)
                load_swiglu(2 * pair + 1, 1)
                load_shared(pair)

            def load_geglu(b):
                chunks = GEGLU_TILES // CHUNK
                for k in range(TOP_K):
                    e = expert(b, k)
                    for q in range(chunks):
                        n = chunks * k + q
                        sp.wait_ge(ring_lo_done, own_no(GEGLU, b, CHUNK * (n + 1)) - CHUNK * RAW_SLOTS)
                        sp.dma_start(raw_chunk[:, n % RAW_SLOTS, :], geglu_w_in[e, q])\
                          .then_inc(raw_landed[n % RAW_SLOTS], 16)
                        if n == 5 and not is_at(b, 0):
                            store(b - 1)

            def store(b):
                sp.wait_ge(mix_added, sample_no(1, b) + 1)
                sp.dma_start(out[b], x[:, b]).then_inc(stored, 16)

            load_geglu(0)
            with sp.Fori(1, BATCH) as b:
                load_geglu(b)
            store(LAST)
            sp.wait_ge(stored, 16 * BATCH)

        @block.gpsimd
        def _(pool):
            with pool.Fori(0, GEGLU_TILES // CHUNK) as i:
                pool.wait_ge(shared_landed, 16 * (i + 1))
                pool.tensor_copy(shared_hi[:, i, :], raw_chunk[:, RAW_SLOTS, :]).then_inc(shared_hi_done, 1)
                pool.wait_ge(shared_hi_done, i + 1)
                pool.tensor_tensor(shared_lo[:, i, :], raw_chunk[:, RAW_SLOTS, :],
                                   shared_hi[:, i, :].bitcast(F32), ALU.subtract).then_inc(shared_lo_done, 1)

        @block.tensor
        def _(pe):
            def three_passes(acc, w_hi, w_lo, x_hi, x_lo, start, stop):
                pe.matmul(acc, w_hi, x_hi, start=start, stop=False)
                pe.matmul(acc, w_hi, x_lo, start=False, stop=False)
                return pe.matmul(acc, w_lo, x_hi, start=False, stop=stop)

            def weights(layer, j, part):
                if is_shared(layer, j):
                    t = j // 3
                    at = (t % CHUNK) * TILE_W + part
                    return (shared_hi[:, t // CHUNK, at:at + P], shared_lo[:, t // CHUNK, at:at + P])
                slot = own_index(layer, j) % RING
                return ring_hi[:, slot, part:part + P], ring_lo[:, slot, part:part + P]

            def hidden_products(layer, b, parity, j):
                t = tile_no(layer, b, j)
                if is_shared(layer, j):
                    if is_at(b, 0) and j == 2:
                        pe.wait_ge(shared_lo_done, GEGLU_TILES // CHUNK)
                else:
                    pe.wait_ge(ring_lo_done, own_no(layer, b, own_index(layer, j)) + 1)
                if j == 0:
                    pe.wait_ge(xs_lo_done, sample_no(layer, b) + 1)
                for n, (bank, done, freed) in enumerate(((ps_first, first_done, gated_done),
                                                         (ps_second, second_done, hidden_done))):
                    wait(pe, freed, t - 1)
                    for c in range(CT):
                        last = three_passes(bank[:, j % 2, :], *weights(layer, j, (n * CT + c) * P),
                                            xs_hi[:, parity, c, :], xs_lo[:, parity, c, :],
                                            start=c == 0, stop=c == CT - 1)
                    last.then_inc(done, 1)

            def down_product(layer, b, j):
                pe.wait_ge(hid_lo_done, tile_no(layer, b, j) + 1)
                if j == 0:
                    wait(pe, out_added, sample_no(layer, b))
                for m in range(CT):
                    last = three_passes(ps_out[:, m, :], *weights(layer, j, (2 * CT + m) * P),
                                        hidden_hi[:, j % 2, :], hidden_lo[:, j % 2, :],
                                        start=j == 0, stop=j == TILES[layer] - 1)
                last.then_inc(down_done, 1)

            def mixed_linear(layer, b):
                n = sample_no(layer, b)
                pe.wait_ge(mix_lo, n + 1)
                wait(pe, mix_added, n)
                for m in range(CT):
                    for c in range(CT):
                        last = three_passes(ps_mix[:, m, :], wm_hi[:, c, m * P:(m + 1) * P],
                                            wm_lo[:, c, m * P:(m + 1) * P], xm_hi[:, c, :], xm_lo[:, c, :],
                                            start=c == 0, stop=c == CT - 1)
                last.then_inc(mix_done, 1)

            def lora_pair(pair):
                pe.wait_ge(lora_scaled, pair + 1)
                pe.wait_ge(mix_added, BATCH)
                wait(pe, lora_ready, pair)
                for c in range(CT):
                    last = pe.matmul(ps_mix[:, c, :], lora_a[:, c * P:(c + 1) * P],
                                     lora_b_scaled.rearrange("p c d -> p (c d)"), start=True, stop=True)
                last.then_inc(lora_made, 1)

            pe.wait_ge(mixer_ready, 1)
            quarter = DIM // GROUP // 4
            for g in range(OWN_GROUPS):
                q, c = divmod(g, CT)
                pe.wait_ge(mix_w_landed[q], 16)
                wait(pe, own_ready, g - 3)
                bank = (ps_first, ps_second)[g % 2][:, g // 2 % 2, :]
                for r in range(quarter):
                    last = pe.matmul(bank[:, r * P:(r + 1) * P], mix_w[:, q * quarter + r, c * P:(c + 1) * P],
                                     mixer[:, :, :].rearrange("p b s -> p (b s)"), start=True, stop=True)
                last.then_inc(own_made, 1)
            mixed_linear(0, 0)
            pe.wait_ge(own_ready, OWN_GROUPS)
            hidden_products(SWIGLU, 0, 0, 0)

            def walk(layer, b, parity):
                for j in range(TILES[layer]):
                    following = ahead(layer, b, parity, j, 1)
                    if following:
                        hidden_products(*following)
                    if layer == SWIGLU and j == 1 and not is_at(b, LAST):
                        mixed_linear(0, b + 1)
                    if layer == GEGLU and j == 4 and not is_at(b, 0):
                        mixed_linear(1, b - 1)
                    if layer == GEGLU and is_at(b, 0) and j % 3 == 2 and j // 3 < LORA_PAIRS:
                        lora_pair(j // 3)
                    down_product(layer, b, j)

            for_samples(pe, lambda b, parity: walk(SWIGLU, b, parity))
            for_samples(pe, lambda b, parity: walk(GEGLU, b, parity))
            mixed_linear(1, LAST)

        @block.scalar
        def _(act):
            act.dma_start(cond_rows[:, :], cond_rows_in).then_inc(rows_landed, 16)
            act.dma_start(select[:, :], select_in).then_inc(rows_landed, 16)
            act.dma_start(mask[:, :, :], mask_in).then_inc(mask_landed, 16)
            consts = ((mix_bias[:, :], mix_bias_in), (base_bias[:, :], base_bias_in),
                      (base[:, :, :], base_in), (lora_a[:, :], lora_a_in), (lora_b[:, :], lora_b_in))
            for to, source in consts:
                act.dma_start(to, source).then_inc(consts_landed, 16)

            input_sample = act.alloc_register("input_sample")
            act.wait_ge(route, 2 * BATCH + 1)
            act.activation(soft[:, :, :], soft[:, :, :], ACT.Exp).then_inc(soft_ready, 1)

            def split_mix(layer, b):
                n = sample_no(layer, b)
                wait(act, mix_done, n)
                if layer == 1:
                    act.wait_ge(out_added, sample_no(GEGLU, b) + 1)
                    act.wait_ge(lora_ready, LORA_PAIRS)
                elif isinstance(b, int):
                    act.wait_ge(x_landed[b], 16)
                else:
                    act.wait_ge(x_landed[3], 16)
                if layer == 0 and is_at(b, 1):
                    act.wait_ge(x_landed[2], 16)
                act.activation(wm_hi[:, :, :], own_w[:, :, b, :], ACT.Copy)
                act.activation(xm_hi[:, :, :], x[:, b], ACT.Copy).then_inc(mix_hi, 1)

            def split_input(layer, b, parity):
                act.wait_ge(*((mix_added, b + 1) if layer == SWIGLU else (out_added, b + 1)))
                if layer == GEGLU and is_at(b, 0):
                    act.wait_ge(second_done, tile_no(SWIGLU, BATCH - 1, 0))
                else:
                    wait(act, second_done, tile_no(layer, b - 1, 0))
                if isinstance(b, int):
                    at = b
                else:
                    act.reg_mov(input_sample, b)
                    at = act.snap(input_sample, min_val=0, max_val=LAST)
                act.activation(xs_hi[:, parity], x[:, at], ACT.Copy).then_inc(xs_hi_done, 1)

            def split_weights(layer, b, parity, j):
                s = own_index(layer, j)
                slot, landed = raw_place(layer, b, parity, s)
                act.wait_ge(raw_landed[slot], landed)
                earlier = ring_predecessor(layer, b, s)
                if earlier:
                    act.wait_ge(down_done, tile_no(*earlier) + 1)
                at = (s % CHUNK) * TILE_W
                act.activation(ring_hi[:, s % RING, :], raw_chunk[:, slot, at:at + TILE_W], ACT.Copy)\
                   .then_inc(ring_hi_done, 1)

            def activate(layer, b, j):
                t = tile_no(layer, b, j)
                act.wait_ge(first_done, t + 1)
                wait(act, hidden_done, t - 1)
                if layer == SWIGLU:
                    act.activation(gated[:, j % 2, :], ps_first[:, j % 2, :], ACT.Silu,
                                   bias=swiglu_bias[:, b, j:j + 1]).then_inc(gated_done, 1)
                else:
                    act.activation(gated[:, j % 2, :], ps_first[:, j % 2, :], ACT.Gelu_apprx_tanh)\
                       .then_inc(gated_done, 1)

            def split_hidden(layer, b, j):
                t = tile_no(layer, b, j)
                act.wait_ge(hidden_done, t + 1)
                wait(act, down_done, t - 1)
                act.activation(hidden_hi[:, j % 2, :], hidden[:, j % 2, :], ACT.Copy).then_inc(hid_hi_done, 1)

            def walk(layer, b, parity):
                for j in range(TILES[layer]):
                    activate(layer, b, j)
                    if layer == SWIGLU and j == 2:
                        if is_at(b, LAST):
                            split_input(GEGLU, 0, 0)
                        else:
                            split_input(SWIGLU, b + 1, 1 - parity)
                    if layer == GEGLU and j == 8 and not is_at(b, LAST):
                        split_input(GEGLU, b + 1, 1 - parity)
                    if layer == GEGLU and j == 1 and not is_at(b, 0):
                        split_mix(1, b - 1)
                    split_hidden(layer, b, j)
                    coming = ahead(layer, b, parity, j, 2)
                    if coming and not is_shared(coming[0], coming[3]):
                        split_weights(*coming)
                    if layer == SWIGLU and j == 0 and not is_at(b, LAST):
                        split_mix(0, b + 1)

            act.wait_ge(own_ready, OWN_GROUPS)
            split_mix(0, 0)
            split_weights(SWIGLU, 0, 0, 0)
            split_input(SWIGLU, 0, 0)
            split_weights(SWIGLU, 0, 0, 1)
            act.wait_ge(bias_landed, 16 * BATCH)
            for layer in (SWIGLU, GEGLU):
                for_samples(act, lambda b, parity: walk(layer, b, parity))
            split_mix(1, LAST)

        @block.vector
        def _(dve):
            steps = [0]

            def routed(instruction):
                steps[0] += 1
                instruction.then_inc(route, 1)
                dve.wait_ge(route, steps[0])

            dve.wait_ge(cond_landed, 16)
            for b in range(BATCH):
                routed(dve.max(ranked[:, b, :], cond[:, b, :]))
                routed(dve.max_index(ranks[:, b, :], ranked[:, b, :], cond[:, b, :]))
            best = ranked[:, :, 0:1].broadcast_to([P, BATCH, EXPERTS])
            routed(dve.tensor_tensor(soft[:, :, :], ranked[:, :, :], best, ALU.subtract))
            dve.wait_ge(rows_landed, 32)
            dve.tensor_tensor(mixer[:, :, :], cond_rows[:, :].unsqueeze(2).broadcast_to([P, BATCH, GROUP]),
                              select[:, :].unsqueeze(1).broadcast_to([P, BATCH, GROUP]), ALU.mult)\
               .then_inc(mixer_ready, 1)
            dve.wait_ge(soft_ready, 1)
            routed(dve.tensor_reduce(total[:, :], soft[:, :, :], AX_X, ALU.add))
            routed(dve.reciprocal(total[:, :], total[:, :]))
            two = [P, BATCH, TOP_K]
            routed(dve.tensor_tensor(top_w[:, :, :], soft[:, :, 0:TOP_K],
                                     total[:, :].unsqueeze(2).broadcast_to(two), ALU.mult))
            routed(dve.tensor_reduce(total[:, :], top_w[:, :, :], AX_X, ALU.add))
            routed(dve.reciprocal(total[:, :], total[:, :]))
            routed(dve.tensor_tensor(top_w[:, :, :], top_w[:, :, :],
                                     total[:, :].unsqueeze(2).broadcast_to(two), ALU.mult))
            scale = 1.0 / NUM_MOE_LAYERS
            routed(dve.tensor_scalar(top_part[:, :, :], top_w[:, :, :], 1.0 - scale, None, ALU.mult))
            routed(dve.scalar_tensor_tensor(out=top_w[:, :, :], in0=top_w[:, :, :], scalar=scale,
                                            in1=top_part[:, :, :], op0=ALU.mult, op1=ALU.add))

            def rest(out_lo, whole, hi):
                return dve.tensor_tensor(out_lo, whole, hi.bitcast(F32), ALU.subtract)

            def split_mix(layer, b):
                dve.wait_ge(mix_hi, sample_no(layer, b) + 1)
                rest(wm_lo[:, :, :], own_w[:, :, b, :], wm_hi[:, :, :])
                rest(xm_lo[:, :, :], x[:, b], xm_hi[:, :, :]).then_inc(mix_lo, 1)

            def split_input(layer, b, parity):
                dve.wait_ge(xs_hi_done, sample_no(layer, b) + 1)
                rest(xs_lo[:, parity], x[:, b], xs_hi[:, parity]).then_inc(xs_lo_done, 1)

            def split_weights(layer, b, parity, j):
                s = own_index(layer, j)
                dve.wait_ge(ring_hi_done, own_no(layer, b, s) + 1)
                slot, _ = raw_place(layer, b, parity, s)
                at = (s % CHUNK) * TILE_W
                rest(ring_lo[:, s % RING, :], raw_chunk[:, slot, at:at + TILE_W], ring_hi[:, s % RING, :])\
                    .then_inc(ring_lo_done, 1)

            def add_mix(layer, b):
                dve.wait_ge(mix_done, sample_no(layer, b) + 1)
                bias = (mix_bias, base_bias)[layer]
                for m in range(CT):
                    last = dve.scalar_tensor_tensor(out=x[:, b, m, :], in0=ps_mix[:, m, :],
                                                    scalar=bias[:, m:m + 1], in1=x[:, b, m, :],
                                                    op0=ALU.add, op1=ALU.add)
                last.then_inc(mix_added, 1)

            def add_out(layer, b):
                dve.wait_ge(down_done, tile_no(layer, b, TILES[layer]))
                for m in range(CT):
                    if layer == SWIGLU:
                        at = 2 * SWIGLU_TILES + m
                        last = dve.scalar_tensor_tensor(out=x[:, b, m, :], in0=ps_out[:, m, :],
                                                        scalar=swiglu_bias[:, b, at:at + 1],
                                                        in1=x[:, b, m, :], op0=ALU.add, op1=ALU.add)
                    else:
                        last = dve.tensor_tensor(x[:, b, m, :], ps_out[:, m, :], x[:, b, m, :], ALU.add)
                last.then_inc(out_added, 1)

            def make_hidden(layer, b, j):
                t = tile_no(layer, b, j)
                dve.wait_ge(second_done, t + 1)
                dve.wait_ge(gated_done, t + 1)
                second, gate, to = ps_second[:, j % 2, :], gated[:, j % 2, :], hidden[:, j % 2, :]
                if is_shared(layer, j):
                    last = dve.tensor_tensor(to, second, gate, ALU.mult)
                elif layer == GEGLU:
                    k = own_index(layer, j) // GEGLU_TILES
                    last = dve.scalar_tensor_tensor(out=to, in0=second, scalar=top_w[:, b, k:k + 1],
                                                    in1=gate, op0=ALU.mult, op1=ALU.mult)
                else:
                    at = SWIGLU_TILES + j
                    last = dve.scalar_tensor_tensor(out=to, in0=second, scalar=swiglu_bias[:, b, at:at + 1],
                                                    in1=gate, op0=ALU.add, op1=ALU.mult)
                last.then_inc(hidden_done, 1)

            def split_hidden(layer, b, j):
                dve.wait_ge(hid_hi_done, tile_no(layer, b, j) + 1)
                rest(hidden_lo[:, j % 2, :], hidden[:, j % 2, :], hidden_hi[:, j % 2, :])\
                    .then_inc(hid_lo_done, 1)

            def scale_lora(pair):
                wait(dve, lora_made, pair)
                for n in range(2):
                    b = 2 * pair + n
                    last = dve.tensor_scalar(lora_b_scaled[:, n, :], lora_b[:, :], cond_rows[:, b:b + 1],
                                             LORA_SCALING, ALU.mult, ALU.mult)
                last.then_inc(lora_scaled, 1)

            def add_base(pair):
                dve.wait_ge(lora_made, pair + 1)
                for c in range(CT):
                    last = dve.tensor_tensor(
                        own_w[:, c, 2 * pair:2 * pair + 2, :],
                        ps_mix[:, c, :].rearrange("p (b d) -> p b d", b=2),
                        base[:, c, :].unsqueeze(1).broadcast_to([P, 2, DIM]), ALU.add)
                last.then_inc(lora_ready, 1)

            def walk(layer, b, parity):
                for j in range(TILES[layer]):
                    make_hidden(layer, b, j)
                    if layer == SWIGLU and j == 2:
                        if is_at(b, LAST):
                            split_input(GEGLU, 0, 0)
                        else:
                            split_input(SWIGLU, b + 1, 1 - parity)
                    if layer == GEGLU and j == 8 and not is_at(b, LAST):
                        split_input(GEGLU, b + 1, 1 - parity)
                    if layer == GEGLU and j == 1 and not is_at(b, 0):
                        split_mix(1, b - 1)
                    split_hidden(layer, b, j)
                    if j == 0:
                        if not is_at(b, 0):
                            add_out(layer, b - 1)
                        elif layer == GEGLU:
                            add_out(SWIGLU, LAST)
                    coming = ahead(layer, b, parity, j, 2)
                    if coming and not is_shared(coming[0], coming[3]):
                        split_weights(*coming)
                    if layer == SWIGLU and not is_at(b, LAST):
                        if j == 0:
                            split_mix(0, b + 1)
                        if j == 1:
                            add_mix(0, b + 1)
                    if layer == GEGLU:
                        if is_at(b, 0) and j < 3 * LORA_PAIRS:
                            if j % 3 == 0:
                                scale_lora(j // 3)
                            if j % 3 == 2:
                                add_base(j // 3)
                        if not is_at(b, 0) and j == 5:
                            add_mix(1, b - 1)

            dve.wait_ge(mask_landed, 16)
            quarter = DIM // GROUP // 4
            for g in range(OWN_GROUPS):
                q, c = divmod(g, CT)
                dve.wait_ge(own_made, g + 1)
                bank = (ps_first, ps_second)[g % 2][:, g // 2 % 2, :]
                rows = slice(q * quarter * GROUP, (q + 1) * quarter * GROUP)
                dve.tensor_tensor(
                    own_w[:, c, :, rows].rearrange("p b (r s) -> p r b s", s=GROUP),
                    bank.rearrange("p (r b s) -> p r b s", r=quarter, b=BATCH),
                    mask[:, c, rows].rearrange("p (r s) -> p r s", s=GROUP).unsqueeze(2)
                    .broadcast_to([P, quarter, BATCH, GROUP]), ALU.mult).then_inc(own_ready, 1)
            dve.wait_ge(consts_landed, 16 * 5)
            split_mix(0, 0)
            add_mix(0, 0)
            split_weights(SWIGLU, 0, 0, 0)
            split_input(SWIGLU, 0, 0)
            split_weights(SWIGLU, 0, 0, 1)
            for layer in (SWIGLU, GEGLU):
                for_samples(dve, lambda b, parity: walk(layer, b, parity))
            add_out(GEGLU, LAST)
            split_mix(1, LAST)
            add_mix(1, LAST)


def kernel(x, cond_8, L0_cond_weight, L0_cond_mask, L0_cond_bias, L1_cond_W_up, L1_cond_b_up,
           L1_cond_W_gate, L1_cond_b_gate, L1_cond_W_down, L1_cond_b_down, L2_cond_skill_gate,
           L2_cond_skill_up, L2_cond_skill_down, L2_cond_shared_gate, L2_cond_shared_up,
           L2_cond_shared_down, L3_cond_W_base, L3_cond_b_base, L3_cond_As, L3_cond_Bs):
    import concourse.bacc as bacc
    import numpy as np
    from concourse.bass_utils import run_bass_kernel_spmd

    def rows_to_partitions(a):
        a = a.reshape(*a.shape[:-2], a.shape[-2] // P, P, a.shape[-1])
        return np.moveaxis(a, -3, -2)

    def chunks(first, second, down):
        e, h, _ = first.shape
        tiles = h // P
        sides = [a.reshape(e, tiles, P, CT, P).transpose(0, 1, 4, 3, 2).reshape(e, tiles, P, CT * P)
                 for a in (first, second)]
        packed = np.concatenate([*sides, down.reshape(e, tiles, P, DIM)], axis=-1)
        packed = packed.reshape(e, tiles // CHUNK, CHUNK, P, TILE_W).transpose(0, 1, 3, 2, 4)
        return packed.reshape(e, tiles // CHUNK, P, CHUNK * TILE_W)

    def columns(a):
        return np.swapaxes(a.reshape(*a.shape[:-1], -1, P), -1, -2)

    a = {k: np.asarray(v) for k, v in locals().items() if k == "x" or k.startswith(("cond", "L"))}
    w = a["L0_cond_weight"]
    arrays = {
        "x_in": rows_to_partitions(a["x"].transpose(0, 2, 1)),
        "cond_in": np.broadcast_to(a["cond_8"], (P, BATCH, EXPERTS)),
        "cond_rows_in": np.repeat(a["cond_8"].T, GROUP, axis=0),
        "select_in": np.tile(np.eye(GROUP, dtype=np.float32), (EXPERTS, 1)),
        "mix_w_in": w.reshape(EXPERTS, DIM // GROUP, GROUP, DIM).transpose(0, 2, 1, 3)
                     .reshape(P, DIM // GROUP, DIM),
        "mask_in": rows_to_partitions(a["L0_cond_mask"].T),
        "mix_bias_in": columns(a["L0_cond_bias"]),
        "swiglu_w_in": chunks(a["L1_cond_W_up"], a["L1_cond_W_gate"],
                              a["L1_cond_W_down"].transpose(0, 2, 1)),
        "swiglu_bias_in": np.concatenate([columns(a[k]) for k in (
            "L1_cond_b_up", "L1_cond_b_gate", "L1_cond_b_down")], axis=-1),
        "geglu_w_in": chunks(a["L2_cond_skill_gate"].transpose(0, 2, 1),
                             a["L2_cond_skill_up"].transpose(0, 2, 1), a["L2_cond_skill_down"]),
        "shared_w_in": chunks(a["L2_cond_shared_gate"].T[None], a["L2_cond_shared_up"].T[None],
                              a["L2_cond_shared_down"][None])[0],
        "base_in": rows_to_partitions(a["L3_cond_W_base"].T),
        "base_bias_in": columns(a["L3_cond_b_base"]),
        "lora_a_in": a["L3_cond_As"].reshape(P, DIM),
        "lora_b_in": a["L3_cond_Bs"].transpose(0, 2, 1).reshape(P, DIM),
    }
    arrays = {k: np.ascontiguousarray(v) for k, v in arrays.items()}
    nc = bacc.Bacc("TRN2", target_bir_lowering=False, num_devices=1)
    args = {k: nc.dram_tensor(k, v.shape, F32, kind="ExternalInput").ap() for k, v in arrays.items()}
    out = nc.dram_tensor("out", (BATCH, P, CT, TOKENS), F32, kind="ExternalOutput").ap()
    build(nc, out=out, **args)
    got = run_bass_kernel_spmd(nc, [arrays], core_ids=[0]).results[0]["out"]
    return got.transpose(0, 3, 2, 1).reshape(BATCH, TOKENS, DIM)
```

```python
from contextlib import ExitStack

import concourse.bass as bass
from concourse import mybir

P = 128
BATCH, TOKENS, DIM = 8, 512, 256
EXPERTS = 8
CT = DIM // P
TOP_K = 2
SWIGLU_TILES = 512 // P
GEGLU_TILES = 1024 // P
TILE_W = 2 * CT * P + DIM
CHUNK = 2
RAW_SLOTS = 4
RING = 4
GROUP = P // EXPERTS
LORA_R = 16
LORA_SCALING = 32.0 / LORA_R
N_BIAS = 2 * SWIGLU_TILES + CT
NUM_MOE_LAYERS = 12
LAST = BATCH - 1

F32 = mybir.dt.float32
F32R = mybir.dt.float32r
U32 = mybir.dt.uint32
ALU = mybir.AluOpType
ACT = mybir.ActivationFunctionType
AX_X = mybir.AxisListType.X

SWIGLU, GEGLU = 0, 1
TILES = (SWIGLU_TILES, (TOP_K + 1) * GEGLU_TILES)
OWN = (SWIGLU_TILES, TOP_K * GEGLU_TILES)


def is_shared(layer, j):
    return layer == GEGLU and j % 3 == 2


def own_index(layer, j):
    return j if layer == SWIGLU else j - j // 3


def tile_no(layer, b, j):
    return TILES[SWIGLU] * b + j if layer == SWIGLU else TILES[SWIGLU] * BATCH + TILES[GEGLU] * b + j


def own_no(layer, b, s):
    return OWN[SWIGLU] * b + s if layer == SWIGLU else OWN[SWIGLU] * BATCH + OWN[GEGLU] * b + s


def sample_no(layer, b):
    return BATCH * layer + b


def is_at(b, n):
    return isinstance(b, int) and b == n


def ahead(layer, b, parity, j, k):
    j += k
    if j < TILES[layer]:
        return layer, b, parity, j
    j -= TILES[layer]
    if not is_at(b, LAST):
        return layer, b + 1, 1 - parity, j
    return (GEGLU, 0, 0, j) if layer == SWIGLU else None


def ring_predecessor(layer, b, s):
    s -= RING
    if s < 0:
        if is_at(b, 0):
            if layer == SWIGLU:
                return None
            layer, b = SWIGLU, LAST
        else:
            b = b - 1
        s += OWN[layer]
    j = s if layer == SWIGLU else s + s // 2
    return layer, b, j


def raw_place(layer, b, parity, s):
    n = s // CHUNK
    if layer == SWIGLU:
        return OWN[SWIGLU] // CHUNK * parity + n, 16 // 2 * (b - parity) + 16
    rounds = OWN[GEGLU] // CHUNK // RAW_SLOTS
    return n % RAW_SLOTS, 16 * (BATCH // 2 + n // RAW_SLOTS + 1 + rounds * b)


def wait(engine, semaphore, value):
    if isinstance(value, int) and value <= 0:
        return
    engine.wait_ge(semaphore, value)


def for_samples(engine, step):
    step(0, 0)
    with engine.Fori(0, (BATCH - 2) // 2) as i:
        step(2 * i + 1, 1)
        step(2 * i + 2, 0)
    step(LAST, LAST % 2)


def build(nc, x_in, cond_in, mixer_parts_in, mix_w_in, mask_in, mix_bias_in, swiglu_w_in,
          swiglu_bias_in, geglu_w_in, shared_w_in, base_in, base_bias_in, lora_a_in, lora_b_in, out):
    with ExitStack() as ctx:
        def sb(name, shape, dt=F32):
            return ctx.enter_context(nc.sbuf_tensor(name, shape, dt))

        def sem(name):
            return ctx.enter_context(nc.semaphore(name))

        x = sb("x", [P, BATCH, CT, TOKENS])
        xs_hi = sb("xs_hi", [P, 2, CT, TOKENS], F32R)
        xs_lo = sb("xs_lo", [P, 2, CT, TOKENS], F32R)
        xm_hi = sb("xm_hi", [P, CT, TOKENS], F32R)
        xm_lo = sb("xm_lo", [P, CT, TOKENS], F32R)
        raw = sb("raw", [P, (RAW_SLOTS + 1) * CHUNK * TILE_W])
        raw_chunk = raw[:, :].rearrange("p (c w) -> p c w", w=CHUNK * TILE_W)
        mix_w_cols = DIM // GROUP * DIM
        mix_w = raw[:, (RAW_SLOTS + 1) * CHUNK * TILE_W - mix_w_cols:].rearrange("p (c t) -> p c t", t=DIM)
        ring_hi = sb("ring_hi", [P, RING, TILE_W], F32R)
        ring_lo = sb("ring_lo", [P, RING, TILE_W], F32R)
        shared_hi = sb("shared_hi", [P, GEGLU_TILES // CHUNK, CHUNK * TILE_W], F32R)
        shared_lo = sb("shared_lo", [P, GEGLU_TILES // CHUNK, CHUNK * TILE_W], F32R)
        own_w = sb("own_w", [P, CT, BATCH, DIM])
        wm_hi = sb("wm_hi", [P, CT, DIM], F32R)
        wm_lo = sb("wm_lo", [P, CT, DIM], F32R)
        gated = sb("gated", [P, 2, TOKENS])
        hidden = sb("hidden", [P, 2, TOKENS])
        hidden_hi = sb("hidden_hi", [P, 2, TOKENS], F32R)
        hidden_lo = sb("hidden_lo", [P, 2, TOKENS], F32R)
        mask = sb("mask", [P, CT, DIM])
        lora_b_scaled = mask[:, :, :]
        base = sb("base", [P, CT, DIM])
        lora_a = sb("lora_a", [P, DIM])
        lora_b = sb("lora_b", [P, DIM])
        mixer_parts = sb("mixer_parts", [P, BATCH + GROUP])
        cond_rows = mixer_parts[:, 0:BATCH]
        select = mixer_parts[:, BATCH:]
        table_warmer = sb("table_warmer", [P, 1])
        mixer = sb("mixer", [P, BATCH, GROUP])
        mix_bias = sb("mix_bias", [P, CT])
        base_bias = sb("base_bias", [P, CT])
        swiglu_bias = sb("swiglu_bias", [P, BATCH, N_BIAS])
        cond = sb("cond", [P, BATCH, EXPERTS])
        ranked = sb("ranked", [P, BATCH, EXPERTS])
        ranks = sb("ranks", [P, BATCH, EXPERTS], U32)
        soft = sb("soft", [P, BATCH, EXPERTS])
        total = sb("total", [P, BATCH])
        top_w = sb("top_w", [P, BATCH, TOP_K])
        top_part = sb("top_part", [P, BATCH, TOP_K])

        ps_first, ps_second, ps_out, ps_mix = (
            ctx.enter_context(nc.psum_tensor(name, [P, 2, TOKENS], F32))
            for name in ("ps_first", "ps_second", "ps_out", "ps_mix"))

        cond_landed, mixer_parts_landed, mask_landed, linear_bias_landed, lora_landed = map(
            sem, ("cond_landed", "mixer_parts_landed", "mask_landed", "linear_bias_landed", "lora_landed"))
        mix_w_landed = [sem(f"mix_w_landed{i}") for i in range(4)]
        x_landed = [sem(f"x_landed{i}") for i in range(4)]
        bias_landed = [sem(f"bias_landed{i}") for i in range(2)]
        raw_landed = [sem(f"raw_landed{i}") for i in range(RAW_SLOTS)]
        shared_landed = sem("shared_landed")
        stored = sem("stored")
        route = sem("route")
        soft_ready = sem("soft_ready")
        mixer_ready = sem("mixer_ready")
        own_made = sem("own_made")
        own_ready = sem("own_ready")
        lora_scaled = sem("lora_scaled")
        lora_made = sem("lora_made")
        lora_ready = sem("lora_ready")
        wm_hi_done, wm_lo_done, xm_hi_done, xm_lo_done, mix_done, mix_added = map(
            sem, ("wm_hi_done", "wm_lo_done", "xm_hi_done", "xm_lo_done", "mix_done", "mix_added"))
        xs_hi_done, xs_lo_done, out_done, out_added = map(
            sem, ("xs_hi_done", "xs_lo_done", "out_done", "out_added"))
        first_done, second_done, gated_done, hidden_done, hid_hi_done, hid_lo_done, down_done = map(
            sem, ("first_done", "second_done", "gated_done", "hidden_done", "hid_hi_done",
                  "hid_lo_done", "down_done"))
        ring_hi_done, ring_lo_done = map(sem, ("ring_hi_done", "ring_lo_done"))
        shared_hi_done, shared_lo_done = map(sem, ("shared_hi_done", "shared_lo_done"))

        LORA_PAIRS = BATCH // 2
        OWN_GROUPS = CT * 4
        block = ctx.enter_context(nc.Block())

        @block.sync
        def _(sp):
            sp.dma_start(cond[:, :, :], cond_in).then_inc(cond_landed, 16)
            quarter = DIM // GROUP // 4
            for i in range(4):
                sp.dma_start(mix_w[:, quarter * i:quarter * (i + 1), :],
                             mix_w_in[:, quarter * i:quarter * (i + 1), :]).then_inc(mix_w_landed[i], 16)
                if i == 0:
                    sp.dma_start(mask[:, :, :], mask_in).then_inc(mask_landed, 16)
            sp.dma_start(x[:, 0], x_in[0]).then_inc(x_landed[0], 16)

            def expert(b, k):
                return sp.value_load(ranks[0:1, b, k:k + 1], min_val=0, max_val=EXPERTS - 1)

            def load_swiglu(b, half):
                e = expert(b, 0)
                wait(sp, bias_landed[half], 16 // 2 * (b - half))
                sp.dma_start(swiglu_bias[:, b, :], swiglu_bias_in[e]).then_inc(bias_landed[half], 16)
                for q in range(SWIGLU_TILES // CHUNK):
                    slot = (SWIGLU_TILES // CHUNK) * half + q
                    wait(sp, ring_lo_done, own_no(SWIGLU, b, CHUNK * (q + 1)) - CHUNK * RAW_SLOTS)
                    sp.dma_start(raw_chunk[:, slot, :], swiglu_w_in[e, q]).then_inc(raw_landed[slot], 16)

            def load_shared(i):
                wait(sp, shared_lo_done, i)
                sp.dma_start(raw_chunk[:, RAW_SLOTS, :], shared_w_in[i]).then_inc(shared_landed, 16)

            sp.wait_ge(route, 2 * BATCH)
            load_swiglu(0, 0)
            sp.dma_start(x[:, 1], x_in[1]).then_inc(x_landed[1], 16)
            sp.dma_start(x[:, 2], x_in[2]).then_inc(x_landed[2], 16)
            sp.wait_ge(own_made, OWN_GROUPS)
            load_swiglu(1, 1)
            sp.dma_start(x[:, 3:], x_in[3:].rearrange("b p c t -> p b c t")).then_inc(x_landed[3], 16)
            for to, source in ((base[:, :, :], base_in), (lora_a[:, :], lora_a_in), (lora_b[:, :], lora_b_in)):
                sp.dma_start(to, source).then_inc(lora_landed, 16)
            load_shared(0)
            with sp.Fori(1, BATCH // 2) as pair:
                load_swiglu(2 * pair, 0)
                load_swiglu(2 * pair + 1, 1)
                load_shared(pair)

            def load_geglu(b):
                chunks = GEGLU_TILES // CHUNK
                for k in range(TOP_K):
                    e = expert(b, k)
                    for q in range(chunks):
                        n = chunks * k + q
                        sp.wait_ge(ring_lo_done, own_no(GEGLU, b, CHUNK * (n + 1)) - CHUNK * RAW_SLOTS)
                        sp.dma_start(raw_chunk[:, n % RAW_SLOTS, :], geglu_w_in[e, q])\
                          .then_inc(raw_landed[n % RAW_SLOTS], 16)
                        if n == 5 and not is_at(b, 0):
                            store(b - 1)

            def store(b):
                sp.wait_ge(mix_added, CT * sample_no(1, b) + CT)
                sp.dma_start(out[b], x[:, b]).then_inc(stored, 16)

            load_geglu(0)
            with sp.Fori(1, BATCH) as b:
                load_geglu(b)
            for m in range(CT):
                sp.wait_ge(mix_added, CT * sample_no(1, LAST) + m + 1)
                sp.dma_start(out[LAST, :, m, :], x[:, LAST, m, :]).then_inc(stored, 16)
            sp.wait_ge(stored, 16 * (LAST + CT))

        @block.gpsimd
        def _(pool):
            with pool.Fori(0, GEGLU_TILES // CHUNK) as i:
                pool.wait_ge(shared_landed, 16 * (i + 1))
                pool.tensor_copy(shared_hi[:, i, :], raw_chunk[:, RAW_SLOTS, :]).then_inc(shared_hi_done, 1)
                pool.wait_ge(shared_hi_done, i + 1)
                pool.tensor_tensor(shared_lo[:, i, :], raw_chunk[:, RAW_SLOTS, :],
                                   shared_hi[:, i, :].bitcast(F32), ALU.subtract).then_inc(shared_lo_done, 1)

        @block.tensor
        def _(pe):
            def three_passes(acc, w_hi, w_lo, x_hi, x_lo, start, stop):
                pe.matmul(acc, w_hi, x_hi, start=start, stop=False)
                pe.matmul(acc, w_hi, x_lo, start=False, stop=False)
                return pe.matmul(acc, w_lo, x_hi, start=False, stop=stop)

            def weights(layer, j, part):
                if is_shared(layer, j):
                    t = j // 3
                    at = (t % CHUNK) * TILE_W + part
                    return (shared_hi[:, t // CHUNK, at:at + P], shared_lo[:, t // CHUNK, at:at + P])
                slot = own_index(layer, j) % RING
                return ring_hi[:, slot, part:part + P], ring_lo[:, slot, part:part + P]

            def hidden_products(layer, b, parity, j):
                t = tile_no(layer, b, j)
                if is_shared(layer, j):
                    if is_at(b, 0) and j == 2:
                        pe.wait_ge(shared_lo_done, GEGLU_TILES // CHUNK)
                else:
                    pe.wait_ge(ring_lo_done, own_no(layer, b, own_index(layer, j)) + 1)
                for n, (bank, done, freed) in enumerate(((ps_first, first_done, gated_done),
                                                         (ps_second, second_done, hidden_done))):
                    wait(pe, freed, t - 1)
                    for c in range(CT):
                        if j == 0 and n == 0:
                            pe.wait_ge(xs_lo_done, CT * sample_no(layer, b) + c + 1)
                        last = three_passes(bank[:, j % 2, :], *weights(layer, j, (n * CT + c) * P),
                                            xs_hi[:, parity, c, :], xs_lo[:, parity, c, :],
                                            start=c == 0, stop=c == CT - 1)
                    last.then_inc(done, 1)

            def down_product(layer, b, j):
                pe.wait_ge(hid_lo_done, tile_no(layer, b, j) + 1)
                for m in range(CT):
                    if j == 0:
                        wait(pe, out_added, CT * sample_no(layer, b) + m + 1 - CT)
                    last = three_passes(ps_out[:, m, :], *weights(layer, j, (2 * CT + m) * P),
                                        hidden_hi[:, j % 2, :], hidden_lo[:, j % 2, :],
                                        start=j == 0, stop=j == TILES[layer] - 1)
                    if j == TILES[layer] - 1 and m == 0:
                        last.then_inc(out_done, 1)
                last.then_inc(down_done, 1)

            def mixed_linear(layer, b):
                n = sample_no(layer, b)
                for m in range(CT):
                    pe.wait_ge(wm_lo_done, CT * n + m + 1)
                    wait(pe, mix_added, CT * n + m + 1 - CT)
                    for c in range(CT):
                        if m == 0:
                            pe.wait_ge(xm_lo_done, CT * n + c + 1)
                        last = three_passes(ps_mix[:, m, :], wm_hi[:, c, m * P:(m + 1) * P],
                                            wm_lo[:, c, m * P:(m + 1) * P], xm_hi[:, c, :], xm_lo[:, c, :],
                                            start=c == 0, stop=c == CT - 1)
                    last.then_inc(mix_done, 1)

            def lora_pair(pair):
                if pair == 0:
                    pe.wait_ge(lora_landed, 16 * 3)
                pe.wait_ge(lora_scaled, pair + 1)
                pe.wait_ge(mix_added, CT * BATCH)
                wait(pe, lora_ready, pair)
                for c in range(CT):
                    last = pe.matmul(ps_mix[:, c, :], lora_a[:, c * P:(c + 1) * P],
                                     lora_b_scaled.rearrange("p c d -> p (c d)"), start=True, stop=True)
                last.then_inc(lora_made, 1)

            pe.wait_ge(mixer_ready, 1)
            quarter = DIM // GROUP // 4
            for g in range(OWN_GROUPS):
                q, c = divmod(g, CT)
                pe.wait_ge(mix_w_landed[q], 16)
                wait(pe, own_ready, g - 3)
                bank = (ps_first, ps_second)[g % 2][:, g // 2 % 2, :]
                for r in range(quarter):
                    last = pe.matmul(bank[:, r * P:(r + 1) * P], mix_w[:, q * quarter + r, c * P:(c + 1) * P],
                                     mixer[:, :, :].rearrange("p b s -> p (b s)"), start=True, stop=True)
                last.then_inc(own_made, 1)
            mixed_linear(0, 0)
            pe.wait_ge(own_ready, OWN_GROUPS)
            hidden_products(SWIGLU, 0, 0, 0)

            def walk(layer, b, parity):
                for j in range(TILES[layer]):
                    following = ahead(layer, b, parity, j, 1)
                    if following:
                        hidden_products(*following)
                    if layer == SWIGLU and j == 1 and not is_at(b, LAST):
                        mixed_linear(0, b + 1)
                    if layer == GEGLU and j == 4 and not is_at(b, 0):
                        mixed_linear(1, b - 1)
                    if layer == GEGLU and is_at(b, 0) and j % 3 == 2 and j // 3 < LORA_PAIRS:
                        lora_pair(j // 3)
                    down_product(layer, b, j)

            for_samples(pe, lambda b, parity: walk(SWIGLU, b, parity))
            for_samples(pe, lambda b, parity: walk(GEGLU, b, parity))
            mixed_linear(1, LAST)

        @block.scalar
        def _(act):
            act.dma_start(mixer_parts[:, :], mixer_parts_in).then_inc(mixer_parts_landed, 16)
            act.dma_start(mix_bias[:, :], mix_bias_in).then_inc(linear_bias_landed, 16)
            act.dma_start(base_bias[:, :], base_bias_in).then_inc(linear_bias_landed, 16)

            input_sample = act.alloc_register("input_sample")
            act.wait_ge(route, 2 * BATCH + 1)
            act.activation(soft[:, :, :], soft[:, :, :], ACT.Exp).then_inc(soft_ready, 1)
            act.wait_ge(mixer_parts_landed, 16)
            act.activation(table_warmer[:, :], mixer_parts[:, 0:1], ACT.Silu)

            def sample_register(b):
                if isinstance(b, int):
                    return b
                act.reg_mov(input_sample, b)
                return act.snap(input_sample, min_val=0, max_val=LAST)

            def split_mix_w(layer, b):
                n = sample_no(layer, b)
                wait(act, mix_done, CT * n)
                if layer == 1 and is_at(b, 0):
                    act.wait_ge(lora_ready, LORA_PAIRS)
                at = sample_register(b)
                act.activation(wm_hi[:, :, :], own_w[:, :, at, :], ACT.Copy).then_inc(wm_hi_done, CT)

            def split_mix_x(layer, b):
                n = sample_no(layer, b)
                if layer == 0:
                    act.wait_ge(x_landed[b if isinstance(b, int) and b < 3 else 3], 16)
                wait(act, mix_done, CT * n)
                for c in range(CT):
                    if layer == 1:
                        act.wait_ge(out_added, CT * sample_no(GEGLU, b) + c + 1)
                    at = sample_register(b)
                    act.activation(xm_hi[:, c, :], x[:, at, c, :], ACT.Copy).then_inc(xm_hi_done, 1)

            def split_input(layer, b, parity):
                if layer == GEGLU and is_at(b, 0):
                    act.wait_ge(second_done, tile_no(SWIGLU, LAST, 0))
                else:
                    wait(act, second_done, tile_no(layer, b - 1, 0))
                for c in range(CT):
                    act.wait_ge((mix_added, out_added)[layer], CT * b + c + 1)
                    at = sample_register(b)
                    act.activation(xs_hi[:, parity, c, :], x[:, at, c, :], ACT.Copy)\
                       .then_inc(xs_hi_done, 1)

            def split_weights(layer, b, parity, j):
                s = own_index(layer, j)
                slot, landed = raw_place(layer, b, parity, s)
                act.wait_ge(raw_landed[slot], landed)
                earlier = ring_predecessor(layer, b, s)
                if earlier:
                    act.wait_ge(down_done, tile_no(*earlier) + 1)
                at = (s % CHUNK) * TILE_W
                act.activation(ring_hi[:, s % RING, :], raw_chunk[:, slot, at:at + TILE_W], ACT.Copy)\
                   .then_inc(ring_hi_done, 1)

            def activate(layer, b, parity, j):
                t = tile_no(layer, b, j)
                if layer == SWIGLU and j == 0:
                    act.wait_ge(bias_landed[parity], 16 // 2 * (b - parity) + 16)
                act.wait_ge(first_done, t + 1)
                wait(act, hidden_done, t - 1)
                if layer == SWIGLU:
                    act.activation(gated[:, j % 2, :], ps_first[:, j % 2, :], ACT.Silu,
                                   bias=swiglu_bias[:, b, j:j + 1]).then_inc(gated_done, 1)
                else:
                    act.activation(gated[:, j % 2, :], ps_first[:, j % 2, :], ACT.Gelu_apprx_tanh)\
                       .then_inc(gated_done, 1)

            def split_hidden(layer, b, j):
                t = tile_no(layer, b, j)
                act.wait_ge(hidden_done, t + 1)
                wait(act, down_done, t - 1)
                act.activation(hidden_hi[:, j % 2, :], hidden[:, j % 2, :], ACT.Copy).then_inc(hid_hi_done, 1)

            def walk(layer, b, parity):
                for j in range(TILES[layer]):
                    activate(layer, b, parity, j)
                    if layer == SWIGLU and j == 2:
                        if is_at(b, LAST):
                            split_input(GEGLU, 0, 0)
                        else:
                            split_input(SWIGLU, b + 1, 1 - parity)
                    if layer == GEGLU and j == 8 and not is_at(b, LAST):
                        split_input(GEGLU, b + 1, 1 - parity)
                    if layer == GEGLU and j == 1 and not is_at(b, 0):
                        split_mix_x(1, b - 1)
                    split_hidden(layer, b, j)
                    coming = ahead(layer, b, parity, j, 2)
                    if coming and not is_shared(coming[0], coming[3]):
                        split_weights(*coming)
                    if layer == SWIGLU and j == 0 and not is_at(b, LAST):
                        split_mix_w(0, b + 1)
                        split_mix_x(0, b + 1)
                    if layer == GEGLU and j == 12:
                        split_mix_w(1, b)

            for m in range(CT):
                if m == 1:
                    split_mix_x(0, 0)
                act.wait_ge(own_ready, OWN_GROUPS // CT * (m + 1))
                columns = slice(m * P, (m + 1) * P)
                act.activation(wm_hi[:, :, columns], own_w[:, :, 0, columns], ACT.Copy)\
                   .then_inc(wm_hi_done, 1)
            split_weights(SWIGLU, 0, 0, 0)
            split_input(SWIGLU, 0, 0)
            split_weights(SWIGLU, 0, 0, 1)
            for_samples(act, lambda b, parity: walk(SWIGLU, b, parity))
            for_samples(act, lambda b, parity: walk(GEGLU, b, parity))
            split_mix_x(1, LAST)

        @block.vector
        def _(dve):
            def routed(instruction):
                steps[0] += 1
                instruction.then_inc(route, 1)
                dve.wait_ge(route, steps[0])

            dve.wait_ge(mixer_parts_landed, 16)
            dve.tensor_tensor(mixer[:, :, :], cond_rows.unsqueeze(2).broadcast_to([P, BATCH, GROUP]),
                              select.unsqueeze(1).broadcast_to([P, BATCH, GROUP]), ALU.mult)\
               .then_inc(mixer_ready, 1)
            dve.wait_ge(cond_landed, 16)
            for b in range(BATCH):
                dve.max(ranked[:, b, :], cond[:, b, :]).then_inc(route, 1)
            for b in range(BATCH):
                dve.wait_ge(route, b + 1)
                dve.max_index(ranks[:, b, :], ranked[:, b, :], cond[:, b, :]).then_inc(route, 1)
            steps = [2 * BATCH]
            best = ranked[:, :, 0:1].broadcast_to([P, BATCH, EXPERTS])
            routed(dve.tensor_tensor(soft[:, :, :], ranked[:, :, :], best, ALU.subtract))

            def normalise():
                dve.wait_ge(soft_ready, 1)
                routed(dve.tensor_reduce(total[:, :], soft[:, :, :], AX_X, ALU.add))
                routed(dve.reciprocal(total[:, :], total[:, :]))
                two = [P, BATCH, TOP_K]
                routed(dve.tensor_tensor(top_w[:, :, :], soft[:, :, 0:TOP_K],
                                         total[:, :].unsqueeze(2).broadcast_to(two), ALU.mult))
                routed(dve.tensor_reduce(total[:, :], top_w[:, :, :], AX_X, ALU.add))
                routed(dve.reciprocal(total[:, :], total[:, :]))
                routed(dve.tensor_tensor(top_w[:, :, :], top_w[:, :, :],
                                         total[:, :].unsqueeze(2).broadcast_to(two), ALU.mult))
                scale = 1.0 / NUM_MOE_LAYERS
                routed(dve.tensor_scalar(top_part[:, :, :], top_w[:, :, :], 1.0 - scale, None, ALU.mult))
                routed(dve.scalar_tensor_tensor(out=top_w[:, :, :], in0=top_w[:, :, :], scalar=scale,
                                                in1=top_part[:, :, :], op0=ALU.mult, op1=ALU.add))

            def rest(out_lo, whole, hi):
                return dve.tensor_tensor(out_lo, whole, hi.bitcast(F32), ALU.subtract)

            def split_mix_w(layer, b):
                dve.wait_ge(wm_hi_done, CT * sample_no(layer, b) + CT)
                rest(wm_lo[:, :, :], own_w[:, :, b, :], wm_hi[:, :, :]).then_inc(wm_lo_done, CT)

            def split_mix_x(layer, b):
                for c in range(CT):
                    dve.wait_ge(xm_hi_done, CT * sample_no(layer, b) + c + 1)
                    rest(xm_lo[:, c, :], x[:, b, c, :], xm_hi[:, c, :]).then_inc(xm_lo_done, 1)

            def split_input(layer, b, parity):
                for c in range(CT):
                    dve.wait_ge(xs_hi_done, CT * sample_no(layer, b) + c + 1)
                    rest(xs_lo[:, parity, c, :], x[:, b, c, :], xs_hi[:, parity, c, :])\
                        .then_inc(xs_lo_done, 1)

            def split_weights(layer, b, parity, j):
                s = own_index(layer, j)
                dve.wait_ge(ring_hi_done, own_no(layer, b, s) + 1)
                slot, _ = raw_place(layer, b, parity, s)
                at = (s % CHUNK) * TILE_W
                rest(ring_lo[:, s % RING, :], raw_chunk[:, slot, at:at + TILE_W], ring_hi[:, s % RING, :])\
                    .then_inc(ring_lo_done, 1)

            def add_mix(layer, b):
                bias = (mix_bias, base_bias)[layer]
                for m in range(CT):
                    dve.wait_ge(mix_done, CT * sample_no(layer, b) + m + 1)
                    dve.scalar_tensor_tensor(out=x[:, b, m, :], in0=ps_mix[:, m, :],
                                             scalar=bias[:, m:m + 1], in1=x[:, b, m, :],
                                             op0=ALU.add, op1=ALU.add).then_inc(mix_added, 1)

            def add_out(layer, b):
                for m in range(CT):
                    if m == 0:
                        dve.wait_ge(out_done, sample_no(layer, b) + 1)
                    else:
                        dve.wait_ge(down_done, tile_no(layer, b, TILES[layer]))
                    if layer == SWIGLU:
                        at = 2 * SWIGLU_TILES + m
                        last = dve.scalar_tensor_tensor(out=x[:, b, m, :], in0=ps_out[:, m, :],
                                                        scalar=swiglu_bias[:, b, at:at + 1],
                                                        in1=x[:, b, m, :], op0=ALU.add, op1=ALU.add)
                    else:
                        last = dve.tensor_tensor(x[:, b, m, :], ps_out[:, m, :], x[:, b, m, :], ALU.add)
                    last.then_inc(out_added, 1)

            def make_hidden(layer, b, j):
                t = tile_no(layer, b, j)
                dve.wait_ge(second_done, t + 1)
                dve.wait_ge(gated_done, t + 1)
                second, gate, to = ps_second[:, j % 2, :], gated[:, j % 2, :], hidden[:, j % 2, :]
                if is_shared(layer, j):
                    last = dve.tensor_tensor(to, second, gate, ALU.mult)
                elif layer == GEGLU:
                    k = own_index(layer, j) // GEGLU_TILES
                    last = dve.scalar_tensor_tensor(out=to, in0=second, scalar=top_w[:, b, k:k + 1],
                                                    in1=gate, op0=ALU.mult, op1=ALU.mult)
                else:
                    at = SWIGLU_TILES + j
                    last = dve.scalar_tensor_tensor(out=to, in0=second, scalar=swiglu_bias[:, b, at:at + 1],
                                                    in1=gate, op0=ALU.add, op1=ALU.mult)
                last.then_inc(hidden_done, 1)

            def split_hidden(layer, b, j):
                dve.wait_ge(hid_hi_done, tile_no(layer, b, j) + 1)
                rest(hidden_lo[:, j % 2, :], hidden[:, j % 2, :], hidden_hi[:, j % 2, :])\
                    .then_inc(hid_lo_done, 1)

            def scale_lora(pair):
                wait(dve, lora_made, pair)
                for n in range(2):
                    b = 2 * pair + n
                    last = dve.tensor_scalar(lora_b_scaled[:, n, :], lora_b[:, :], cond_rows[:, b:b + 1],
                                             LORA_SCALING, ALU.mult, ALU.mult)
                last.then_inc(lora_scaled, 1)

            def add_base(pair):
                dve.wait_ge(lora_made, pair + 1)
                for c in range(CT):
                    last = dve.tensor_tensor(
                        own_w[:, c, 2 * pair:2 * pair + 2, :],
                        ps_mix[:, c, :].rearrange("p (b d) -> p b d", b=2),
                        base[:, c, :].unsqueeze(1).broadcast_to([P, 2, DIM]), ALU.add)
                last.then_inc(lora_ready, 1)

            def walk(layer, b, parity):
                for j in range(TILES[layer]):
                    make_hidden(layer, b, j)
                    split_hidden(layer, b, j)
                    if layer == SWIGLU and j == 2:
                        if is_at(b, LAST):
                            split_input(GEGLU, 0, 0)
                        else:
                            split_input(SWIGLU, b + 1, 1 - parity)
                    if layer == GEGLU and j == 8 and not is_at(b, LAST):
                        split_input(GEGLU, b + 1, 1 - parity)
                    if layer == GEGLU and j == 1 and not is_at(b, 0):
                        split_mix_x(1, b - 1)
                    if j == 0:
                        if not is_at(b, 0):
                            add_out(layer, b - 1)
                        elif layer == GEGLU:
                            add_out(SWIGLU, LAST)
                    coming = ahead(layer, b, parity, j, 2)
                    if coming and not is_shared(coming[0], coming[3]):
                        split_weights(*coming)
                    if layer == SWIGLU and not is_at(b, LAST):
                        if j == 0:
                            split_mix_w(0, b + 1)
                            split_mix_x(0, b + 1)
                        if j == 1:
                            add_mix(0, b + 1)
                    if layer == GEGLU:
                        if is_at(b, 0) and j < 3 * LORA_PAIRS:
                            if j == 0:
                                dve.wait_ge(lora_landed, 16 * 3)
                            if j % 3 == 0:
                                scale_lora(j // 3)
                            if j % 3 == 2:
                                add_base(j // 3)
                        if not is_at(b, 0) and j == 5:
                            add_mix(1, b - 1)
                        if j == 12:
                            split_mix_w(1, b)

            dve.wait_ge(mask_landed, 16)
            quarter = DIM // GROUP // 4
            for g in range(OWN_GROUPS):
                q, c = divmod(g, CT)
                dve.wait_ge(own_made, g + 1)
                bank = (ps_first, ps_second)[g % 2][:, g // 2 % 2, :]
                rows = slice(q * quarter * GROUP, (q + 1) * quarter * GROUP)
                dve.tensor_tensor(
                    own_w[:, c, :, rows].rearrange("p b (r s) -> p r b s", s=GROUP),
                    bank.rearrange("p (r b s) -> p r b s", r=quarter, b=BATCH),
                    mask[:, c, rows].rearrange("p (r s) -> p r s", s=GROUP).unsqueeze(2)
                    .broadcast_to([P, quarter, BATCH, GROUP]), ALU.mult).then_inc(own_ready, 1)
                if g % (OWN_GROUPS // CT) == OWN_GROUPS // CT - 1:
                    m = g // (OWN_GROUPS // CT)
                    columns = slice(m * P, (m + 1) * P)
                    dve.wait_ge(wm_hi_done, m + 1)
                    rest(wm_lo[:, :, columns], own_w[:, :, 0, columns], wm_hi[:, :, columns])\
                        .then_inc(wm_lo_done, 1)
                if g == OWN_GROUPS - 3:
                    split_mix_x(0, 0)
            split_weights(SWIGLU, 0, 0, 0)
            dve.wait_ge(linear_bias_landed, 32)
            add_mix(0, 0)
            split_input(SWIGLU, 0, 0)
            split_weights(SWIGLU, 0, 0, 1)
            normalise()
            for_samples(dve, lambda b, parity: walk(SWIGLU, b, parity))
            for_samples(dve, lambda b, parity: walk(GEGLU, b, parity))
            add_out(GEGLU, LAST)
            split_mix_x(1, LAST)
            add_mix(1, LAST)


def kernel(x, cond_8, L0_cond_weight, L0_cond_mask, L0_cond_bias, L1_cond_W_up, L1_cond_b_up,
           L1_cond_W_gate, L1_cond_b_gate, L1_cond_W_down, L1_cond_b_down, L2_cond_skill_gate,
           L2_cond_skill_up, L2_cond_skill_down, L2_cond_shared_gate, L2_cond_shared_up,
           L2_cond_shared_down, L3_cond_W_base, L3_cond_b_base, L3_cond_As, L3_cond_Bs):
    import concourse.bacc as bacc
    import numpy as np
    from concourse.bass_utils import run_bass_kernel_spmd

    def rows_to_partitions(a):
        a = a.reshape(*a.shape[:-2], a.shape[-2] // P, P, a.shape[-1])
        return np.moveaxis(a, -3, -2)

    def chunks(first, second, down):
        e, h, _ = first.shape
        tiles = h // P
        sides = [a.reshape(e, tiles, P, CT, P).transpose(0, 1, 4, 3, 2).reshape(e, tiles, P, CT * P)
                 for a in (first, second)]
        packed = np.concatenate([*sides, down.reshape(e, tiles, P, DIM)], axis=-1)
        packed = packed.reshape(e, tiles // CHUNK, CHUNK, P, TILE_W).transpose(0, 1, 3, 2, 4)
        return packed.reshape(e, tiles // CHUNK, P, CHUNK * TILE_W)

    def columns(a):
        return np.swapaxes(a.reshape(*a.shape[:-1], -1, P), -1, -2)

    a = {k: np.asarray(v) for k, v in locals().items() if k == "x" or k.startswith(("cond", "L"))}
    w = a["L0_cond_weight"]
    arrays = {
        "x_in": rows_to_partitions(a["x"].transpose(0, 2, 1)),
        "cond_in": np.broadcast_to(a["cond_8"], (P, BATCH, EXPERTS)),
        "mixer_parts_in": np.concatenate([np.repeat(a["cond_8"].T, GROUP, axis=0),
                                          np.tile(np.eye(GROUP, dtype=np.float32), (EXPERTS, 1))], axis=1),
        "mix_w_in": w.reshape(EXPERTS, DIM // GROUP, GROUP, DIM).transpose(0, 2, 1, 3)
                     .reshape(P, DIM // GROUP, DIM),
        "mask_in": rows_to_partitions(a["L0_cond_mask"].T),
        "mix_bias_in": columns(a["L0_cond_bias"]),
        "swiglu_w_in": chunks(a["L1_cond_W_up"], a["L1_cond_W_gate"],
                              a["L1_cond_W_down"].transpose(0, 2, 1)),
        "swiglu_bias_in": np.concatenate([columns(a[k]) for k in (
            "L1_cond_b_up", "L1_cond_b_gate", "L1_cond_b_down")], axis=-1),
        "geglu_w_in": chunks(a["L2_cond_skill_gate"].transpose(0, 2, 1),
                             a["L2_cond_skill_up"].transpose(0, 2, 1), a["L2_cond_skill_down"]),
        "shared_w_in": chunks(a["L2_cond_shared_gate"].T[None], a["L2_cond_shared_up"].T[None],
                              a["L2_cond_shared_down"][None])[0],
        "base_in": rows_to_partitions(a["L3_cond_W_base"].T),
        "base_bias_in": columns(a["L3_cond_b_base"]),
        "lora_a_in": a["L3_cond_As"].reshape(P, DIM),
        "lora_b_in": a["L3_cond_Bs"].transpose(0, 2, 1).reshape(P, DIM),
    }
    arrays = {k: np.ascontiguousarray(v) for k, v in arrays.items()}
    nc = bacc.Bacc("TRN2", target_bir_lowering=False, num_devices=1)
    args = {k: nc.dram_tensor(k, v.shape, F32, kind="ExternalInput").ap() for k, v in arrays.items()}
    out = nc.dram_tensor("out", (BATCH, P, CT, TOKENS), F32, kind="ExternalOutput").ap()
    build(nc, out=out, **args)
    got = run_bass_kernel_spmd(nc, [arrays], core_ids=[0]).results[0]["out"]
    return got.transpose(0, 3, 2, 1).reshape(BATCH, TOKENS, DIM)
```
